# Optimizing a Trainium2 kernel written in Bass

```python
import numpy as np
import jax
import jax.numpy as jnp

def _softmax(x, axis=-1):
    return jax.nn.softmax(x, axis=axis)

def _gelu(x):
    return jax.nn.gelu(x, approximate=True)

def _silu(x):
    return jax.nn.silu(x)

def _sigmoid(x):
    return jax.nn.sigmoid(x)

def _layernorm(x, axis=-1, eps=1e-05):
    m = jnp.mean(x, axis=axis, keepdims=True)
    v = jnp.var(x, axis=axis, keepdims=True)
    return (x - m) / jnp.sqrt(v + eps)

def _scatter_add(tgt, idx, src, axis=0):
    return tgt.at[idx].add(src)

def _segment_sum(src, seg, n):
    return jax.ops.segment_sum(src, seg, n)
kernel_name = 'mk_rec_standalone_d1_rec_r8_05ec71'

def setup_inputs(seed: int=0):
    np.random.seed(seed)
    _w = jnp.asarray

    def _rec_inputs():
        import jax
        import jax.numpy as jnp
        _rk = jax.random.key(seed)
        r_x = -0.000520686 + 1.00062 * jax.random.normal(jax.random.fold_in(_rk, 1), (2048, 256), jnp.float32)
        return r_x
    r_x = _rec_inputs()

    def _L0_rec_setup():
        import jax, jax.numpy as jnp
        import numpy as np
        B, IN, H, OUT, L = (1024, 256, 256, 128, 5)
        ALPHA = 0.5
        key = jax.random.key(seed)
        ks = jax.random.split(key, 8)
        s_in = 1.0 / np.sqrt(IN)
        s_h = 1.0 / np.sqrt(H)
        return {'x': jax.random.normal(ks[0], (B, IN), jnp.float32), 'W_in': jax.random.uniform(ks[1], (H, IN), jnp.float32, -s_in, s_in), 'b_in': jax.random.uniform(ks[2], (H,), jnp.float32, -s_in, s_in), 'Ws': jax.random.normal(ks[3], (L, H, H), jnp.float32) * (0.7 / np.sqrt(H)), 'bs': jax.random.uniform(ks[4], (L, H), jnp.float32, -s_h, s_h), 'scales': jnp.ones((L,), jnp.float32), 'W_head': jax.random.uniform(ks[5], (OUT, H), jnp.float32, -s_h, s_h), 'b_head': jax.random.uniform(ks[6], (OUT,), jnp.float32, -s_h, s_h), 'steps': 30}
    _L0_rec_all = _L0_rec_setup()
    _L0_rec_in = {k: v for k, v in _L0_rec_all.items() if k in ('W_in', 'b_in', 'Ws', 'bs', 'scales', 'W_head', 'b_head')}
    del _L0_rec_all
    return {'r_x': r_x, 'L0_rec_W_in': _L0_rec_in['W_in'], 'L0_rec_b_in': _L0_rec_in['b_in'], 'L0_rec_Ws': _L0_rec_in['Ws'], 'L0_rec_bs': _L0_rec_in['bs'], 'L0_rec_scales': _L0_rec_in['scales'], 'L0_rec_W_head': _L0_rec_in['W_head'], 'L0_rec_b_head': _L0_rec_in['b_head']}

def reference(r_x, L0_rec_W_in, L0_rec_b_in, L0_rec_Ws, L0_rec_bs, L0_rec_scales, L0_rec_W_head, L0_rec_b_head):
    import jax
    import jax.numpy as jnp

    def _L0_rec_ref(x, W_in, b_in, Ws, bs, scales, W_head, b_head, steps):
        import jax, jax.numpy as jnp
        import numpy as np
        B, IN, H, OUT, L = (1024, 256, 256, 128, 5)
        ALPHA = 0.5
        x_emb = x @ W_in.T + b_in
        Wsc = Ws * scales[:, None, None]
        h0 = jnp.zeros((L, x.shape[0], H), x.dtype)

        def step(h, _):
            pre = jnp.concatenate([x_emb[None], h[:-1]], axis=0)
            tgt = jnp.tanh(jnp.einsum('lbi,loi->lbo', pre, Wsc) + bs[:, None, :])
            h_new = (1.0 - ALPHA) * h + ALPHA * tgt
            return (h_new, None)
        h_final, _ = jax.lax.scan(step, h0, None, length=steps)
        return h_final[-1] @ W_head.T + b_head
    y = _L0_rec_ref(r_x, L0_rec_W_in, L0_rec_b_in, L0_rec_Ws, L0_rec_bs, L0_rec_scales, L0_rec_W_head, L0_rec_b_head, 30)
    return y

_drawn_inputs = setup_inputs


def setup_inputs(seed=0):
    import zlib

    import numpy as np

    out = dict(_drawn_inputs(seed))
    spreads = {'L0_rec_scales': (1.0, 0.2)}
    factors = {}
    for name, (base, spread) in spreads.items():
        noise = np.random.default_rng([zlib.crc32(name.encode()), seed]).standard_normal(out[name].shape)
        drawn = base * np.exp(spread * noise) if base else spread * noise
        out[name] = jnp.asarray(drawn.astype(out[name].dtype))
    for name, factor in factors.items():
        out[name] = (out[name] * factor).astype(out[name].dtype)
    return out
```

```python
from contextlib import ExitStack

import concourse.bass as bass
from concourse import mybir


def leaky_tanh_stack(nc: bass.Bass, x, W_in, b_in, Ws, bs, scales, W_head, b_head, y):
    f32, f32r = mybir.dt.float32, mybir.dt.float32r
    ALU, ACT = mybir.AluOpType, mybir.ActivationFunctionType

    P = 128
    ROWS, IN = x.shape
    L, H, _ = Ws.shape
    OUT = W_head.shape[0]
    STEPS = 30
    HB = H // P
    CH = 512
    NCH = ROWS // CH
    TPC = CH // P
    LAST = L - 1
    WAVES = STEPS - LAST
    SEAM = 4
    assert IN == H and OUT == P and LAST == 4 and WAVES % 2 == 0 and SEAM % 2 == 0
    HALF = 0.5
    UP = [2.0 ** (w - WAVES + 1) for w in range(WAVES)]
    DOWN = [2.0 ** (WAVES - 2 - w) for w in range(WAVES)]
    RAMP = [1.0 - 2.0 ** -(w + 1) for w in range(WAVES)]

    ctx = ExitStack()
    with ctx:
        def sb(name, shape, dt=f32):
            return ctx.enter_context(nc.sbuf_tensor(name, shape, dt))

        def sem(name):
            return ctx.enter_context(nc.semaphore(name))

        ident = sb("ident", [P, P])
        w_rows = sb("w_rows", [P, L + 1, HB, H])
        head_rows = sb("head_rows", [P, H])
        bias_rows = sb("bias_rows", [(L + 1) * HB, P])
        bias = sb("bias", [P, L + 1, HB])
        b_head_all = sb("b_head_all", [P, OUT])
        mat_scale = sb("mat_scale", [P, L + 1])
        w_hi = sb("w_hi", [P, L + 1, HB, H], f32r)
        w_lo = sb("w_lo", [P, L + 1, HB, H], f32r)
        w_full = sb("w_full", [P, L + 1, HB, H])
        head_hi = sb("head_hi", [P, HB, OUT], f32r)
        head_lo = sb("head_lo", [P, HB, OUT], f32r)
        x_rows = sb("x_rows", [P, ROWS // P, IN])
        u_sb = sb("u_sb", [P, NCH, HB * CH])
        up_tab = sb("up_tab", [P, WAVES])
        down_tab = sb("down_tab", [P, WAVES])
        ramp_tab = sb("ramp_tab", [P, WAVES])
        g_col = sb("g_col", [P, LAST, HB])
        z_col = sb("z_col", [P, LAST, HB])
        t_col = sb("t_col", [P, LAST, HB])
        h_col = sb("h_col", [P, LAST, HB])
        tgt = [None] + [sb(f"tgt{l}", [P, 2, HB, CH]) for l in range(1, L)]
        t_hi = [None] + [sb(f"t_hi{l}", [P, 2, HB, CH], f32r) for l in range(1, LAST)]
        t_lo = [None] + [sb(f"t_lo{l}", [P, 2, HB, CH], f32r) for l in range(1, LAST)]
        xT_hi, xT_lo, e_hi, e_lo, t0_hi, t0_lo = t_hi[1], t_lo[1], t_hi[2], t_lo[2], t_hi[3], t_lo[3]
        t0 = tgt[3]
        g4 = sb("g4", [P, HB, CH])
        h4_hi = sb("h4_hi", [P, HB, CH], f32r)
        h4_lo = sb("h4_lo", [P, HB, CH], f32r)
        y_sb = sb("y_sb", [P, NCH, TPC, OUT])

        ps = ctx.enter_context(nc.psum_tensor("ps", [P, 8, CH], f32))
        Z_BANK = {2: 2, 3: 4, 4: 6}
        HEAD_BANK, COL_BANK = 0, 1
        XT_BANK, EMB_BANK, T0_BANK, U_BANK = 0, 2, 4, 6
        W_BANK = [2, 4, 6, 3, 5, 7]
        HEADT_BANK, BIAS_BANK = 0, 1

        w_in_sb = [sem(f"w_in_sb{m}") for m in range(L + 1)]
        head_in_sb = sem("head_in_sb")
        bias_in_sb = sem("bias_in_sb")
        scale_in_sb = sem("scale_in_sb")
        b_head_in_sb = sem("b_head_in_sb")
        x_in_sb = [sem(f"x_in_sb{c}") for c in range(NCH)]
        y_stored = sem("y_stored")
        ident_zeroed = sem("ident_zeroed")
        ident_ready = sem("ident_ready")
        const_ready = sem("const_ready")
        tab_step = sem("tab_step")
        bias_T = sem("bias_T")
        bias_ready = sem("bias_ready")
        w_T = sem("w_T")
        w_hi_done = sem("w_hi_done")
        w_full_done = sem("w_full_done")
        w_lo_done = sem("w_lo_done")
        col_mm = sem("col_mm")
        col_z = sem("col_z")
        col_t = sem("col_t")
        col_g = sem("col_g")
        h_col_ready = sem("h_col_ready")
        xT_mm = sem("xT_mm")
        xT_hi_done = sem("xT_hi_done")
        xT_done = sem("xT_done")
        emb_mm = sem("emb_mm")
        e_hi_done = sem("e_hi_done")
        e_done = sem("e_done")
        t0_mm = sem("t0_mm")
        t0_tanh = sem("t0_tanh")
        t0_hi_done = sem("t0_hi_done")
        t0_done = sem("t0_done")
        u_mm = sem("u_mm")
        u_done = sem("u_done")
        tanh_done = [None] + [sem(f"tanh_done{l}") for l in range(1, L)]
        hi_part = [None] + [sem(f"hi_part{l}") for l in range(1, LAST)]
        first_done = sem("first_done")
        split_done = [None] + [sem(f"split_done{l}") for l in range(1, LAST)]
        sum_done = sem("sum_done")
        mm_done = {l: sem(f"mm_done{l}") for l in range(2, L)}
        h4_hi_done = sem("h4_hi_done")
        h4_done = sem("h4_done")
        y_mm = sem("y_mm")
        y_done = sem("y_done")

        def three_passes(out, weights_hi, weights_lo, moving_hi, moving_lo, o):
            return passes(out, weights_hi, weights_lo, moving_hi, moving_lo, o, True)

        def passes(out, weights_hi, weights_lo, moving_hi, moving_lo, o, start):
            cols = slice(o * P, (o + 1) * P)
            ops = []
            for k in range(HB):
                ops += [(weights_hi[:, k, cols], moving_lo[:, k, :]), (weights_hi[:, k, cols], moving_hi[:, k, :]),
                        (weights_lo[:, k, cols], moving_hi[:, k, :])]
            for i, (w, v) in enumerate(ops):
                last = nc.tensor.matmul(out, w, v, start=(start and i == 0), stop=(i == len(ops) - 1),
                                        skip_group_check=True)
            return last

        def wave_number(c, w):
            return c * WAVES + w

        block = ctx.enter_context(nc.Block())

        @block.sync
        def _(sp):
            sp.dma_start(w_rows[:, 0], W_in.rearrange("(b p) i -> p b i", p=P)).then_inc(w_in_sb[0], 16)
            for m in range(1, L + 1, 2):
                sp.dma_start(w_rows[:, m], Ws[m - 1].rearrange("(b p) i -> p b i", p=P)).then_inc(w_in_sb[m], 16)
            sp.dma_start(head_rows[:], W_head).then_inc(head_in_sb, 16)
            for c in range(0, NCH, 2):
                sp.dma_start(x_rows[:, c * TPC:(c + 1) * TPC, :],
                             x[c * CH:(c + 1) * CH, :].rearrange("(n p) i -> p n i", p=P)).then_inc(x_in_sb[c], 16)
            sp.dma_start(b_head_all[:], b_head.rearrange("(a o) -> a o", a=1).broadcast_to([P, OUT])
                         ).then_inc(b_head_in_sb, 16)
            for c in range(NCH):
                sp.wait_ge(y_done, c + 1)
                sp.dma_start(y[c * CH:(c + 1) * CH, :].rearrange("(n p) o -> p n o", p=P),
                             y_sb[:, c]).then_inc(y_stored, 16)
            sp.wait_ge(y_stored, 16 * NCH)

        @block.gpsimd
        def _(pool):
            nc.gpsimd.memset(ident[:], 0.0).then_inc(ident_zeroed, 1)
            pool.wait_ge(ident_zeroed, 1)
            nc.gpsimd.affine_select(out=ident[:], in_=ident[:], compare_op=ALU.not_equal, fill=1.0, base=0,
                                    pattern=[[-1, P]], channel_multiplier=1).then_inc(ident_ready, 1)

        @block.tensor
        def _(pe):
            pe.wait_ge(ident_ready, 1)
            pe.wait_ge(bias_in_sb, 32)
            NB = (L + 1) * HB
            nc.tensor.transpose(ps[:, BIAS_BANK, 0:NB], bias_rows[:], ident[0:NB, 0:NB]).then_inc(bias_T, 1)
            for m in range(L + 1):
                pe.wait_ge(w_in_sb[m], 16)
                for k in range(HB):
                    for o in range(HB):
                        at = k * H + o * P
                        last = nc.tensor.transpose(ps[:, W_BANK[m], at:at + P],
                                                   w_rows[:, m, o, k * P:(k + 1) * P], ident[:])
                last.then_inc(w_T, 1)
            pe.wait_ge(head_in_sb, 16)
            for k in range(HB):
                last = nc.tensor.transpose(ps[:, HEADT_BANK, k * OUT:(k + 1) * OUT],
                                           head_rows[:, k * P:(k + 1) * P], ident[:])
            last.then_inc(w_T, 1)

            pe.wait_ge(bias_ready, 1)
            pe.wait_ge(w_full_done, LAST - 1)
            for r in range(1, LAST):
                pe.wait_ge(col_t, 1) if r == 1 else pe.wait_ge(col_g, r - 1)
                for l in range(r + 1, LAST + 1):
                    for o in range(HB):
                        at = (l - 1) * HB + o
                        for k in range(HB):
                            last = nc.tensor.matmul(ps[:, COL_BANK, at:at + 1],
                                                    w_full[:, 1 + l, k, o * P:(o + 1) * P],
                                                    g_col[:, l - 2, k:k + 1], start=(k == 0), stop=(k == HB - 1))
                last.then_inc(col_mm, 1)

            def transpose_x(c):
                pe.wait_ge(x_in_sb[c], 16)
                if c == 0:
                    pe.wait_ge(w_lo_done, L + 2)
                    pe.wait_ge(col_z, LAST - 1)
                else:
                    pe.wait_ge(xT_done, c)
                for k in range(HB):
                    for n in range(TPC):
                        last = nc.tensor.transpose(ps[:, XT_BANK + k, n * P:(n + 1) * P],
                                                   x_rows[:, c * TPC + n, k * P:(k + 1) * P], ident[:])
                last.then_inc(xT_mm, 1)

            def product(c, m, bank, ready, free, hi, lo, done):
                pe.wait_ge(ready, c + 1)
                if c == 0:
                    pe.wait_ge(w_hi_done, L + 2)
                    pe.wait_ge(w_lo_done, L + 2)
                else:
                    pe.wait_ge(free, c)
                for o in range(HB):
                    last = three_passes(ps[:, bank + o, :], w_hi[:, m], w_lo[:, m], hi[:, c % 2], lo[:, c % 2], o)
                last.then_inc(done, 1)

            for s in range(NCH + 3):
                if 0 <= s - 3:
                    product(s - 3, 2, U_BANK, t0_done, u_done, t0_hi, t0_lo, u_mm)
                if 0 <= s - 2 < NCH:
                    product(s - 2, 1, T0_BANK, e_done, t0_tanh, e_hi, e_lo, t0_mm)
                if 0 <= s - 1 < NCH:
                    product(s - 1, 0, EMB_BANK, xT_done, e_done, xT_hi, xT_lo, emb_mm)
                if s < NCH:
                    transpose_x(s)

            def layer(l, c, w, first, parity):
                n = wave_number(c, w)
                pe.wait_ge(split_done[l - 1], n + 1)
                for o in range(HB):
                    if not (isinstance(n, int) and n == 0):
                        pe.wait_ge(tanh_done[l], 2 * n + o - 1)
                    elif o == 0:
                        pe.wait_ge(u_done, NCH)
                    passes(ps[:, Z_BANK[l] + o, :], w_hi[:, 1 + l], w_lo[:, 1 + l], t_hi[l - 1][:, parity],
                           t_lo[l - 1][:, parity], o, first).then_inc(mm_done[l], 1)

            def seam(prev, nxt):
                for i in range(SEAM):
                    for l in range(2, L):
                        w = i - (l - 2)
                        if w >= 0 and nxt is not None:
                            layer(l, nxt, w, w == 0, w % 2)
                        elif w < 0 and prev is not None:
                            layer(l, prev, w + WAVES, False, w % 2)
                if prev is not None:
                    pe.wait_ge(h4_done, prev + 1)
                    for n in range(TPC):
                        rows = slice(n * P, (n + 1) * P)
                        ops = []
                        for k in range(HB):
                            ops += [(h4_hi[:, k, rows], head_lo[:, k, :]), (h4_hi[:, k, rows], head_hi[:, k, :]),
                                    (h4_lo[:, k, rows], head_hi[:, k, :])]
                        for j, (a, b) in enumerate(ops):
                            last = nc.tensor.matmul(ps[:, HEAD_BANK, n * OUT:(n + 1) * OUT], a, b,
                                                    start=(j == 0), stop=(j == len(ops) - 1))
                    last.then_inc(y_mm, 1)

            def steady(c):
                with pe.Fori(SEAM, WAVES - 1, 2) as m:
                    for i in range(2):
                        for l in range(2, L):
                            layer(l, c, m + (i - (l - 2)), False, (i - (l - 2)) % 2)

            seam(None, 0)
            with pe.Fori(0, NCH - 1) as c:
                steady(c)
                seam(c, c + 1)
            steady(NCH - 1)
            seam(NCH - 1, None)

        @block.scalar
        def _(act):
            act.dma_start(bias_rows[0:HB, :], b_in.rearrange("(b p) -> b p", p=P)).then_inc(bias_in_sb, 16)
            act.dma_start(bias_rows[HB:(L + 1) * HB, :],
                          bs.rearrange("l (b p) -> (l b) p", p=P)).then_inc(bias_in_sb, 16)
            act.dma_start(mat_scale[:, 1:L + 1], scales.rearrange("(a l) -> a l", a=1).broadcast_to([P, L])
                          ).then_inc(scale_in_sb, 16)
            for m in range(2, L + 1, 2):
                act.dma_start(w_rows[:, m], Ws[m - 1].rearrange("(b p) i -> p b i", p=P)).then_inc(w_in_sb[m], 16)
            for c in range(1, NCH, 2):
                act.dma_start(x_rows[:, c * TPC:(c + 1) * TPC, :],
                              x[c * CH:(c + 1) * CH, :].rearrange("(n p) i -> p n i", p=P)).then_inc(x_in_sb[c], 16)

            act.wait_ge(bias_T, 1)
            nc.scalar.copy(bias[:].rearrange("p m b -> p (m b)"), ps[:, BIAS_BANK, 0:(L + 1) * HB]).then_inc(bias_ready, 1)
            act.wait_ge(bias_ready, 1)
            nc.scalar.activation(g_col[:], bias[:, 2:L + 1, :], ACT.Tanh).then_inc(col_t, 1)
            act.wait_ge(scale_in_sb, 16)
            act.wait_ge(const_ready, 1)
            for m in range(L + 1):
                act.wait_ge(w_T, m + 1)
                nc.scalar.mul(w_hi[:, m].rearrange("p k o -> p (k o)"), ps[:, W_BANK[m], :],
                              mat_scale[:, m:m + 1]).then_inc(w_hi_done, 1)
                if m >= 3:
                    nc.scalar.mul(w_full[:, m].rearrange("p k o -> p (k o)"), ps[:, W_BANK[m], :],
                                  mat_scale[:, m:m + 1]).then_inc(w_full_done, 1)
            act.wait_ge(w_T, L + 2)
            nc.scalar.copy(head_hi[:].rearrange("p k o -> p (k o)"),
                           ps[:, HEADT_BANK, 0:HB * OUT]).then_inc(w_hi_done, 1)
            for r in range(1, LAST):
                act.wait_ge(col_z, r)
                nc.scalar.activation(t_col[:, r:LAST, :], z_col[:, r:LAST, :], ACT.Tanh).then_inc(col_t, 1)

            def embed(c):
                act.wait_ge(emb_mm, c + 1)
                if c >= 2:
                    act.wait_ge(t0_mm, c - 1)
                for o in range(HB):
                    nc.scalar.activation(e_hi[:, c % 2, o, :], ps[:, EMB_BANK + o, :], ACT.Identity,
                                         bias=bias[:, 0, o:o + 1]).then_inc(e_hi_done, 1)

            def target0(c):
                act.wait_ge(t0_mm, c + 1)
                if c >= 2:
                    act.wait_ge(t0_done, c - 1)
                for o in range(HB):
                    last = nc.scalar.activation(t0[:, c % 2, o, :], ps[:, T0_BANK + o, :], ACT.Tanh,
                                                bias=bias[:, 1, o:o + 1])
                last.then_inc(t0_tanh, 1)

            def keep_u(c):
                act.wait_ge(u_mm, c + 1)
                nc.scalar.copy(u_sb[:, c, :], ps[:, U_BANK:U_BANK + HB, :].rearrange("p b n -> p (b n)")
                               ).then_inc(u_done, 1)

            for s in range(NCH + 2):
                if 0 <= s - 2:
                    keep_u(s - 2)
                if 0 <= s - 1 < NCH:
                    target0(s - 1)
                if s < NCH:
                    embed(s)

            address = act.alloc_register("address")

            def taken_after_wait(value, least, most):
                act.reg_mov(address, value)
                return act.snap(address, min_val=least, max_val=most)

            def layer(l, c, w, parity):
                n = wave_number(c, w)
                freed = sum_done if l == LAST else split_done[l]
                for o in range(HB):
                    if l > 1:
                        act.wait_ge(mm_done[l], 2 * n + o + 1)
                    if o == 0 and not (isinstance(n, int) and n < 2):
                        act.wait_ge(freed, n - 1)
                    if l == 1:
                        at = c if isinstance(c, int) else taken_after_wait(c, 0, NCH - 1)
                        source = u_sb[:, bass.ds(at, 1), o * CH:(o + 1) * CH].rearrange("p a n -> p (a n)")
                    else:
                        source = ps[:, Z_BANK[l] + o, :]
                    if isinstance(w, int):
                        scale = RAMP[w] if l == 1 else DOWN[w]
                    else:
                        at = taken_after_wait(w, 1, WAVES - 1)
                        scale = (ramp_tab if l == 1 else down_tab)[:, bass.ds(at, 1)]
                    nc.scalar.activation(tgt[l][:, parity, o, :], source, ACT.Tanh, bias=bias[:, 1 + l, o:o + 1],
                                         scale=scale).then_inc(tanh_done[l], 1)

            def seam(prev, nxt):
                for i in range(SEAM):
                    for l in range(1, L):
                        w = i - (l - 1)
                        c, v = (nxt, w) if w >= 0 else (prev, w + WAVES)
                        if c is not None:
                            layer(l, c, v, v % 2)

            def steady(c):
                with act.Fori(SEAM, WAVES - 1, 2) as m:
                    for i in range(2):
                        for l in range(1, L):
                            layer(l, c, m + (i - (l - 1)), (i - (l - 1)) % 2)

            act.wait_ge(u_done, NCH)
            seam(None, 0)
            act.wait_ge(tab_step, 3)
            with act.Fori(0, NCH - 1) as c:
                steady(c)
                seam(c, c + 1)
            steady(NCH - 1)
            seam(NCH - 1, None)

        @block.vector
        def _(dve):
            nc.vector.memset(mat_scale[:, 0:1], 1.0).then_inc(const_ready, 1)
            for w in range(WAVES):
                last = nc.vector.memset(up_tab[:, w:w + 1], UP[w])
            last.then_inc(tab_step, 1)
            for w in range(WAVES):
                last = nc.vector.memset(down_tab[:, w:w + 1], DOWN[w])
            last.then_inc(tab_step, 1)
            for w in range(WAVES):
                last = nc.vector.memset(ramp_tab[:, w:w + 1], RAMP[w])
            last.then_inc(tab_step, 1)

            dve.wait_ge(const_ready, 1)
            dve.wait_ge(scale_in_sb, 16)
            for m in range(L + 1):
                dve.wait_ge(w_hi_done, m + 1)
                if m >= 3:
                    dve.wait_ge(w_full_done, m - 2)
                nc.vector.scalar_tensor_tensor(
                    out=w_lo[:, m].rearrange("p k o -> p (k o)"), in0=ps[:, W_BANK[m], :], scalar=mat_scale[:, m:m + 1],
                    in1=w_hi[:, m].rearrange("p k o -> p (k o)").bitcast(f32), op0=ALU.mult,
                    op1=ALU.subtract).then_inc(w_lo_done, 1)
            dve.wait_ge(w_hi_done, L + 2)
            nc.vector.tensor_tensor(head_lo[:].rearrange("p k o -> p (k o)"), ps[:, HEADT_BANK, 0:HB * OUT],
                                    head_hi[:].rearrange("p k o -> p (k o)").bitcast(f32),
                                    ALU.subtract).then_inc(w_lo_done, 1)

            dve.wait_ge(bias_ready, 1)
            for r in range(1, LAST):
                dve.wait_ge(col_mm, r)
                nc.vector.scalar_tensor_tensor(
                    out=z_col[:, r:LAST, :].rearrange("p l b -> p (l b)"), in0=ps[:, COL_BANK, r * HB:LAST * HB],
                    scalar=HALF, in1=bias[:, r + 2:L + 1, :].rearrange("p l b -> p (l b)"), op0=ALU.mult,
                    op1=ALU.add).then_inc(col_z, 1)
                dve.wait_ge(col_t, r + 1)
                nc.vector.scalar_tensor_tensor(out=g_col[:, r:LAST, :], in0=g_col[:, r:LAST, :], scalar=HALF,
                                               in1=t_col[:, r:LAST, :], op0=ALU.mult, op1=ALU.add).then_inc(col_g, 1)
            dve.wait_ge(col_g, LAST - 1)
            nc.vector.tensor_scalar(h_col[:], g_col[:], HALF, None, ALU.mult).then_inc(h_col_ready, 1)

            def split_x(c):
                dve.wait_ge(xT_mm, c + 1)
                if c >= 2:
                    dve.wait_ge(emb_mm, c - 1)
                both = ps[:, XT_BANK:XT_BANK + HB, :]
                nc.vector.tensor_copy(xT_hi[:, c % 2], both).then_inc(xT_hi_done, 1)
                dve.wait_ge(xT_hi_done, c + 1)
                nc.vector.tensor_tensor(xT_lo[:, c % 2], both, xT_hi[:, c % 2].bitcast(f32),
                                        ALU.subtract).then_inc(xT_done, 1)

            def split_embedding(c):
                for o in range(HB):
                    dve.wait_ge(e_hi_done, HB * c + o + 1)
                    last = nc.vector.scalar_tensor_tensor(
                        out=e_lo[:, c % 2, o, :], in0=ps[:, EMB_BANK + o, :], scalar=bias[:, 0, o:o + 1],
                        in1=e_hi[:, c % 2, o, :].bitcast(f32), op0=ALU.add, op1=ALU.subtract)
                last.then_inc(e_done, 1)

            def split_t0(c):
                dve.wait_ge(t0_tanh, c + 1)
                if c >= 2:
                    dve.wait_ge(u_mm, c - 1)
                nc.vector.tensor_copy(t0_hi[:, c % 2], t0[:, c % 2]).then_inc(t0_hi_done, 1)
                dve.wait_ge(t0_hi_done, c + 1)
                nc.vector.tensor_tensor(t0_lo[:, c % 2], t0[:, c % 2], t0_hi[:, c % 2].bitcast(f32),
                                        ALU.subtract).then_inc(t0_done, 1)

            for s in range(NCH + 2):
                if 0 <= s - 2:
                    split_t0(s - 2)
                if 0 <= s - 1 < NCH:
                    split_embedding(s - 1)
                if s < NCH:
                    split_x(s)

            dve.wait_ge(h_col_ready, 1)
            dve.wait_ge(tab_step, 3)

            def split(l, c, w, up, first, parity):
                n = wave_number(c, w)
                t = tgt[l][:, parity]
                dve.wait_ge(tanh_done[l], 2 * n + 2)
                if isinstance(n, int) and n < 2:
                    if n == 0 and l == 1:
                        dve.wait_ge(u_mm, NCH)
                else:
                    dve.wait_ge(mm_done[l + 1], 2 * n - 2)
                if first:
                    for o in range(HB):
                        last = nc.vector.tensor_scalar(t[:, o, :], t[:, o, :], h_col[:, l - 1, o:o + 1], None, ALU.add)
                    last.then_inc(first_done, 1)
                    dve.wait_ge(first_done, c * (LAST - 1) + l)
                nc.vector.tensor_scalar(t_hi[l][:, parity], t, up, None, ALU.mult).then_inc(hi_part[l], 1)
                dve.wait_ge(hi_part[l], n + 1)
                nc.vector.scalar_tensor_tensor(out=t_lo[l][:, parity], in0=t, scalar=up,
                                               in1=t_hi[l][:, parity].bitcast(f32), op0=ALU.mult,
                                               op1=ALU.subtract).then_inc(split_done[l], 1)

            def add_target(c, w, up, first, parity):
                n = wave_number(c, w)
                t = tgt[LAST][:, parity]
                dve.wait_ge(tanh_done[LAST], 2 * n + 2)
                if first:
                    if not (isinstance(c, int) and c == 0):
                        dve.wait_ge(h4_done, c)
                    for o in range(HB):
                        last = nc.vector.tensor_scalar(g4[:, o, :], t[:, o, :], h_col[:, LAST - 1, o:o + 1], up,
                                                       ALU.add, ALU.mult)
                    last.then_inc(sum_done, 1)
                else:
                    dve.wait_ge(sum_done, n)
                    nc.vector.scalar_tensor_tensor(out=g4[:], in0=t, scalar=up, in1=g4[:], op0=ALU.mult,
                                                   op1=ALU.add).then_inc(sum_done, 1)

            def seam(prev, nxt):
                for i in range(SEAM):
                    for l in range(1, L):
                        w = i - (l - 1)
                        c, v = (nxt, w) if w >= 0 else (prev, w + WAVES)
                        if l == LAST and i == SEAM - 1 and prev is not None:
                            dve.wait_ge(sum_done, wave_number(prev, WAVES))
                            nc.vector.tensor_scalar(h4_hi[:], g4[:], HALF, None, ALU.mult).then_inc(h4_hi_done, 1)
                            dve.wait_ge(h4_hi_done, prev + 1)
                            nc.vector.scalar_tensor_tensor(out=h4_lo[:], in0=g4[:], scalar=HALF, in1=h4_hi[:].bitcast(f32),
                                                           op0=ALU.mult, op1=ALU.subtract).then_inc(h4_done, 1)
                        if c is not None:
                            if l == LAST:
                                add_target(c, v, UP[v], v == 0, v % 2)
                            else:
                                split(l, c, v, UP[v], v == 0, v % 2)

            def write_y(c):
                dve.wait_ge(y_mm, c + 1)
                nc.vector.tensor_tensor(y_sb[:, bass.ds(c, 1)].rearrange("p a n o -> p (a n) o"), ps[:, HEAD_BANK, :].rearrange("p (n o) -> p n o", o=OUT),
                                        b_head_all[:].unsqueeze(1).broadcast_to([P, TPC, OUT]),
                                        ALU.add).then_inc(y_done, 1)

            def steady(c):
                with dve.Fori(SEAM, WAVES - 1, 2) as m:
                    for i in range(2):
                        for l in range(1, L):
                            w = m + (i - (l - 1))
                            up = up_tab[:, bass.ds(w, 1)]
                            if l == LAST:
                                add_target(c, w, up, False, (i - (l - 1)) % 2)
                            else:
                                split(l, c, w, up, False, (i - (l - 1)) % 2)

            dve.wait_ge(b_head_in_sb, 16)
            seam(None, 0)
            with dve.Fori(0, NCH - 1) as c:
                steady(c)
                seam(c, c + 1)
                write_y(c)
            steady(NCH - 1)
            seam(NCH - 1, None)
            write_y(NCH - 1)


_INS = ['r_x', 'L0_rec_W_in', 'L0_rec_b_in', 'L0_rec_Ws', 'L0_rec_bs', 'L0_rec_scales', 'L0_rec_W_head', 'L0_rec_b_head']
_OUTS = [((2048, 128), 'float32')]


def kernel(**inputs):
    import numpy as _np
    import concourse.bacc as _bacc
    from concourse import mybir as _mybir
    from concourse.bass_utils import run_bass_kernel_spmd as _run

    nc = _bacc.Bacc("TRN2", target_bir_lowering=False, num_devices=1)
    arrays, args = {}, []
    for name in _INS:
        a = _np.ascontiguousarray(inputs[name])
        arrays[f"in_{name}_dram"] = a
        args.append(nc.dram_tensor(f"in_{name}_dram", a.shape, _mybir.dt.from_np(a.dtype), kind="ExternalInput").ap())
    for i, (shape, dtype) in enumerate(_OUTS):
        dt = _mybir.dt.from_np(_np.dtype(dtype))
        args.append(nc.dram_tensor(f"out_{i}_dram", shape, dt, kind="ExternalOutput").ap())
    leaky_tanh_stack(nc, *args)
    r = _run(nc, [arrays], core_ids=[0])
    return r.results[0]["out_0_dram"]
```

```python
from contextlib import ExitStack

import concourse.bass as bass
from concourse import mybir


def leaky_tanh_stack(nc: bass.Bass, x, W_in, b_in, Ws, bs, scales, W_head, b_head, y):
    f32, f32r = mybir.dt.float32, mybir.dt.float32r
    ALU, ACT = mybir.AluOpType, mybir.ActivationFunctionType

    P = 128
    ROWS, IN = x.shape
    L, H, _ = Ws.shape
    OUT = W_head.shape[0]
    STEPS = 30
    HB = H // P
    CH = 512
    NCH = ROWS // CH
    TPC = CH // P
    LAST = L - 1
    WAVES = STEPS - LAST
    SEAM = 6
    AHEAD = 6
    LAGS = LAST - 1
    assert IN == H and OUT == P and LAST == 4 and WAVES % 2 == 0 and SEAM % 2 == 0
    HALF = 0.5
    UP = [2.0 ** (w - WAVES + 1) for w in range(WAVES)]
    DOWN = [2.0 ** (WAVES - 2 - w) for w in range(WAVES)]
    RAMP = [1.0 - 2.0 ** -(w + 1) for w in range(WAVES)]

    ctx = ExitStack()
    with ctx:
        def sb(name, shape, dt=f32):
            return ctx.enter_context(nc.sbuf_tensor(name, shape, dt))

        def sem(name):
            return ctx.enter_context(nc.semaphore(name))

        ident = sb("ident", [P, P])
        w_in_rows = sb("w_in_rows", [P, HB, IN])
        w_rows = sb("w_rows", [P, L, HB, H])
        head_rows = sb("head_rows", [P, H])
        bias_rows = sb("bias_rows", [(L + 1) * HB, P])
        bias = sb("bias", [P, L + 1, HB])
        b_head_all = sb("b_head_all", [P, OUT])
        a_bias = sb("a_bias", [P, HB])
        w_scale = sb("w_scale", [P, L])
        w_hi = sb("w_hi", [P, L, HB, H], f32r)
        w_lo = sb("w_lo", [P, L, HB, H], f32r)
        w_full = sb("w_full", [P, L, HB, H])
        head_hi = sb("head_hi", [P, HB, OUT], f32r)
        head_lo = sb("head_lo", [P, HB, OUT], f32r)
        x_rows = sb("x_rows", [P, TPC, IN])
        xT_hi = sb("xT_hi", [P, HB, CH], f32r)
        xT_lo = sb("xT_lo", [P, HB, CH], f32r)
        t0 = sb("t0", [P, HB, CH])
        t0_hi = sb("t0_hi", [P, HB, CH], f32r)
        t0_lo = sb("t0_lo", [P, HB, CH], f32r)
        u_sb = sb("u_sb", [P, HB, CH])
        up_tab = sb("up_tab", [P, WAVES])
        down_tab = sb("down_tab", [P, WAVES])
        ramp_tab = sb("ramp_tab", [P, WAVES])
        g_col = sb("g_col", [P, LAST, HB])
        z_col = sb("z_col", [P, LAST, HB])
        t_col = sb("t_col", [P, LAST, HB])
        h_col = sb("h_col", [P, LAST, HB])
        tgt = [None] + [sb(f"tgt{l}", [P, 2, HB, CH]) for l in range(1, L)]
        t_hi = [None] + [sb(f"t_hi{l}", [P, 2, HB, CH], f32r) for l in range(1, LAST)]
        t_lo = [None] + [sb(f"t_lo{l}", [P, 2, HB, CH], f32r) for l in range(1, LAST)]
        g4 = sb("g4", [P, HB, CH])
        h4_hi = sb("h4_hi", [P, HB, CH], f32r)
        h4_lo = sb("h4_lo", [P, HB, CH], f32r)
        y_sb = sb("y_sb", [P, NCH, TPC, OUT])

        ps = ctx.enter_context(nc.psum_tensor("ps", [P, 8, CH], f32))
        Z_BANK = {2: 2, 3: 4, 4: 6}
        HEAD_BANK = 0
        SETUP_BANK = 0
        BIAS_BANK, A_BANK, HEADT_BANK = 2, 4, 4
        W_BANK = [3, 5, 6, 7, 3]
        A_BIAS_AT = 64
        COL_BANK = 1

        w_rows_in = [sem(f"w_rows_in{l}") for l in range(L)]
        w_in_rows_in = sem("w_in_rows_in")
        head_rows_in = sem("head_rows_in")
        bias_rows_in = sem("bias_rows_in")
        scale_in = sem("scale_in")
        b_head_in = sem("b_head_in")
        x_in = sem("x_in")
        y_stored = sem("y_stored")
        ident_zeroed = sem("ident_zeroed")
        ident_ready = sem("ident_ready")
        tab_step = sem("tab_step")
        bias_T = sem("bias_T")
        bias_ready = sem("bias_ready")
        w_T = [sem(f"w_T{l}") for l in range(L)]
        head_T = sem("head_T")
        w_full_done = [sem(f"w_full_done{l}") for l in range(L)]
        w_hi_done = [sem(f"w_hi_done{l}") for l in range(L)]
        w_lo_done = [sem(f"w_lo_done{l}") for l in range(L)]
        head_hi_done = sem("head_hi_done")
        head_lo_done = sem("head_lo_done")
        a_mm = sem("a_mm")
        a_bias_done = sem("a_bias_done")
        col_mm = sem("col_mm")
        col_z = sem("col_z")
        col_t = sem("col_t")
        col_g = sem("col_g")
        h_col_ready = sem("h_col_ready")
        xT_mm = sem("xT_mm")
        xT_hi_done = sem("xT_hi_done")
        xT_done = sem("xT_done")
        t0_mm = sem("t0_mm")
        t0_tanh = sem("t0_tanh")
        t0_hi_done = sem("t0_hi_done")
        t0_done = sem("t0_done")
        u_mm = sem("u_mm")
        u_done = sem("u_done")
        tanh_done = [None] + [sem(f"tanh_done{l}") for l in range(1, L)]
        hi_part = [None] + [sem(f"hi_part{l}") for l in range(1, LAST)]
        first_done = sem("first_done")
        split_done = [None] + [sem(f"split_done{l}") for l in range(1, LAST)]
        sum_done = sem("sum_done")
        mm_done = {l: sem(f"mm_done{l}") for l in range(2, L)}
        h4_hi_done = sem("h4_hi_done")
        h4_done = sem("h4_done")
        y_mm = sem("y_mm")
        y_done = sem("y_done")

        def passes(out, weights_hi, weights_lo, moving_hi, moving_lo, o, start):
            cols = slice(o * P, (o + 1) * P)
            ops = []
            for k in range(HB):
                ops += [(weights_hi[:, k, cols], moving_lo[:, k, :]), (weights_hi[:, k, cols], moving_hi[:, k, :]),
                        (weights_lo[:, k, cols], moving_hi[:, k, :])]
            for i, (w, v) in enumerate(ops):
                last = nc.tensor.matmul(out, w, v, start=(start and i == 0), stop=(i == len(ops) - 1),
                                        skip_group_check=True)
            return last

        def wave_number(c, w):
            return c * WAVES + w

        block = ctx.enter_context(nc.Block())

        @block.sync
        def _(sp):
            def load_matrix(l):
                sp.dma_start(w_rows[:, l], Ws[l].rearrange("(b p) i -> p b i", p=P)).then_inc(w_rows_in[l], 16)

            def load_x(c):
                if c > 0:
                    sp.wait_ge(xT_mm, c)
                sp.dma_start(x_rows[:], x[c * CH:(c + 1) * CH, :].rearrange("(n p) i -> p n i", p=P)).then_inc(x_in, 16)

            def store_y(c):
                sp.wait_ge(y_done, c + 1)
                sp.dma_start(y[c * CH:(c + 1) * CH, :].rearrange("(n p) o -> p n o", p=P),
                             y_sb[:, c]).then_inc(y_stored, 16)

            load_matrix(0)
            load_x(0)
            load_matrix(2)
            load_matrix(4)
            sp.dma_start(b_head_all[:], b_head.rearrange("(a o) -> a o", a=1).broadcast_to([P, OUT])
                         ).then_inc(b_head_in, 16)
            load_x(1)
            for c in range(NCH):
                if c + 2 < NCH:
                    load_x(c + 2)
                store_y(c)
            sp.wait_ge(y_stored, 16 * NCH)

        @block.gpsimd
        def _(pool):
            nc.gpsimd.memset(ident[:], 0.0).then_inc(ident_zeroed, 1)
            pool.wait_ge(ident_zeroed, 1)
            nc.gpsimd.affine_select(out=ident[:], in_=ident[:], compare_op=ALU.not_equal, fill=1.0, base=0,
                                    pattern=[[-1, P]], channel_multiplier=1).then_inc(ident_ready, 1)

        @block.tensor
        def _(pe):
            def transpose_matrix(l):
                pe.wait_ge(w_rows_in[l], 16)
                for k in range(HB):
                    for o in range(HB):
                        at = k * H + o * P
                        last = nc.tensor.transpose(ps[:, W_BANK[l], at:at + P],
                                                   w_rows[:, l, o, k * P:(k + 1) * P], ident[:])
                last.then_inc(w_T[l], 1)

            def shared_columns(r):
                pe.wait_ge(col_t, 1) if r == 1 else pe.wait_ge(col_g, r - 1)
                for l in range(r + 1, LAST + 1):
                    for o in range(HB):
                        at = (l - 1) * HB + o
                        for k in range(HB):
                            last = nc.tensor.matmul(ps[:, COL_BANK, at:at + 1],
                                                    w_full[:, l, k, o * P:(o + 1) * P],
                                                    g_col[:, l - 2, k:k + 1], start=(k == 0), stop=(k == HB - 1))
                last.then_inc(col_mm, 1)

            def transpose_x(c):
                pe.wait_ge(x_in, 16 * c + 16)
                for k in range(HB):
                    for n in range(TPC):
                        last = nc.tensor.transpose(ps[:, SETUP_BANK + k, n * P:(n + 1) * P],
                                                   x_rows[:, n, k * P:(k + 1) * P], ident[:])
                last.then_inc(xT_mm, 1)

            def product_t0(c):
                pe.wait_ge(xT_done, c + 1)
                for o in range(HB):
                    last = passes(ps[:, SETUP_BANK + o, :], w_hi[:, 0], w_lo[:, 0], xT_hi, xT_lo, o, True)
                last.then_inc(t0_mm, 1)

            def product_u(c):
                pe.wait_ge(t0_done, c + 1)
                for o in range(HB):
                    last = passes(ps[:, SETUP_BANK + o, :], w_hi[:, 1], w_lo[:, 1], t0_hi, t0_lo, o, True)
                last.then_inc(u_mm, 1)

            pe.wait_ge(ident_ready, 1)
            pe.wait_ge(bias_rows_in, 32)
            NB = (L + 1) * HB
            nc.tensor.transpose(ps[:, BIAS_BANK, 0:NB], bias_rows[:], ident[0:NB, 0:NB]).then_inc(bias_T, 1)
            transpose_matrix(0)
            transpose_x(0)
            transpose_matrix(1)
            pe.wait_ge(w_full_done[0], 1)
            pe.wait_ge(w_in_rows_in, 16)
            for i in range(HB):
                for k in range(HB):
                    last = nc.tensor.matmul(ps[:, A_BANK, i * H:(i + 1) * H], w_in_rows[:, k, i * P:(i + 1) * P],
                                            w_full[:, 0, k, :], start=(k == 0), stop=(k == HB - 1))
            last.then_inc(a_mm, 1)
            pe.wait_ge(bias_ready, 1)
            for o in range(HB):
                for k in range(HB):
                    last = nc.tensor.matmul(ps[:, BIAS_BANK, A_BIAS_AT + o:A_BIAS_AT + o + 1],
                                            w_full[:, 0, k, o * P:(o + 1) * P], bias[:, 0, k:k + 1],
                                            start=(k == 0), stop=(k == HB - 1))
            last.then_inc(a_mm, 1)
            transpose_matrix(2)
            transpose_matrix(3)
            pe.wait_ge(w_lo_done[0], 1)
            product_t0(0)
            transpose_matrix(4)
            pe.wait_ge(head_rows_in, 16)
            for k in range(HB):
                last = nc.tensor.transpose(ps[:, HEADT_BANK, k * OUT:(k + 1) * OUT],
                                           head_rows[:, k * P:(k + 1) * P], ident[:])
            last.then_inc(head_T, 1)
            pe.wait_ge(w_lo_done[1], 1)
            product_u(0)
            for l in range(2, L):
                pe.wait_ge(w_full_done[l], 1)
            pe.wait_ge(u_done, 1)
            shared_columns(1)
            pe.wait_ge(a_bias_done, 1)
            for l in range(2, L):
                pe.wait_ge(w_lo_done[l], 1)
            pe.wait_ge(head_lo_done, 1)

            def layer(l, c, w, first, parity):
                n = wave_number(c, w)
                pe.wait_ge(split_done[l - 1], n + 1)
                for o in range(HB):
                    if not (isinstance(n, int) and n == 0):
                        pe.wait_ge(tanh_done[l], 2 * n + o - 1)
                    passes(ps[:, Z_BANK[l] + o, :], w_hi[:, l], w_lo[:, l], t_hi[l - 1][:, parity],
                           t_lo[l - 1][:, parity], o, first).then_inc(mm_done[l], 1)

            def head(c):
                for k in range(HB):
                    pe.wait_ge(h4_done, HB * c + k + 1)
                    for n in range(TPC):
                        rows = slice(n * P, (n + 1) * P)
                        ops = [(h4_hi[:, k, rows], head_lo[:, k, :]), (h4_hi[:, k, rows], head_hi[:, k, :]),
                               (h4_lo[:, k, rows], head_hi[:, k, :])]
                        for j, (a, b) in enumerate(ops):
                            last = nc.tensor.matmul(ps[:, HEAD_BANK, n * OUT:(n + 1) * OUT], a, b,
                                                    start=(k == 0 and n == 0 and j == 0),
                                                    stop=(k == HB - 1 and j == len(ops) - 1), skip_group_check=True)
                last.then_inc(y_mm, 1)

            def seam(prev, nxt):
                for i in range(SEAM if nxt is not None else LAGS):
                    for l in range(2, L):
                        w = i - (l - 2)
                        if w >= 0 and nxt is not None:
                            layer(l, nxt, w, w == 0, w % 2)
                        elif w < 0 and prev is not None:
                            layer(l, prev, w + WAVES, False, w % 2)
                    if prev is None and i + 2 < LAST:
                        shared_columns(i + 2)
                    if i == LAGS and prev is not None:
                        head(prev)
                if nxt is None:
                    head(prev)

            def steady(c, end):
                with pe.Fori(SEAM, end - 1, 2) as m:
                    for i in range(2):
                        for l in range(2, L):
                            layer(l, c, m + (i - (l - 2)), False, (i - (l - 2)) % 2)

            def ahead(c):
                for i in range(AHEAD):
                    for l in range(2, L):
                        w = WAVES - AHEAD + i - (l - 2)
                        layer(l, c, w, False, w % 2)
                    if i == 0:
                        transpose_x(c + 1)
                    elif i == 2:
                        product_t0(c + 1)
                    elif i == 4:
                        product_u(c + 1)

            seam(None, 0)
            with pe.Fori(0, NCH - 1) as c:
                steady(c, WAVES - AHEAD)
                ahead(c)
                seam(c, c + 1)
            steady(NCH - 1, WAVES)
            seam(NCH - 1, None)

        @block.scalar
        def _(act):
            act.dma_start(bias_rows[0:HB, :], b_in.rearrange("(b p) -> b p", p=P)).then_inc(bias_rows_in, 16)
            act.dma_start(bias_rows[HB:(L + 1) * HB, :],
                          bs.rearrange("l (b p) -> (l b) p", p=P)).then_inc(bias_rows_in, 16)
            act.dma_start(w_scale[:], scales.rearrange("(a l) -> a l", a=1).broadcast_to([P, L])).then_inc(scale_in, 16)
            act.dma_start(w_in_rows[:], W_in.rearrange("(b p) i -> p b i", p=P)).then_inc(w_in_rows_in, 16)
            act.dma_start(w_rows[:, 1], Ws[1].rearrange("(b p) i -> p b i", p=P)).then_inc(w_rows_in[1], 16)
            act.dma_start(w_rows[:, 3], Ws[3].rearrange("(b p) i -> p b i", p=P)).then_inc(w_rows_in[3], 16)
            act.dma_start(head_rows[:], W_head).then_inc(head_rows_in, 16)

            def scaled(out, l):
                return nc.scalar.mul(out[:, l].rearrange("p k o -> p (k o)"), ps[:, W_BANK[l], :], w_scale[:, l:l + 1])

            def x_high():
                return nc.scalar.copy(xT_hi[:].rearrange("p b n -> p (b n)"),
                                      ps[:, SETUP_BANK:SETUP_BANK + HB, :].rearrange("p b n -> p (b n)")
                                      ).then_inc(xT_hi_done, 1)

            def target0(c):
                act.wait_ge(t0_mm, c + 1)
                for o in range(HB):
                    last = nc.scalar.activation(t0[:, o, :], ps[:, SETUP_BANK + o, :], ACT.Tanh, bias=a_bias[:, o:o + 1])
                last.then_inc(t0_tanh, 1)

            def keep_u(c):
                act.wait_ge(u_mm, c + 1)
                nc.scalar.copy(u_sb[:].rearrange("p b n -> p (b n)"),
                               ps[:, SETUP_BANK:SETUP_BANK + HB, :].rearrange("p b n -> p (b n)")).then_inc(u_done, 1)

            act.wait_ge(bias_T, 1)
            nc.scalar.copy(bias[:].rearrange("p m b -> p (m b)"), ps[:, BIAS_BANK, 0:(L + 1) * HB]).then_inc(bias_ready, 1)
            act.wait_ge(scale_in, 16)
            act.wait_ge(w_T[0], 1)
            scaled(w_full, 0).then_inc(w_full_done[0], 1)
            act.wait_ge(bias_ready, 1)
            nc.scalar.activation(g_col[:], bias[:, 2:L + 1, :], ACT.Tanh).then_inc(col_t, 1)
            act.wait_ge(xT_mm, 1)
            x_high()
            act.wait_ge(a_mm, 1)
            nc.scalar.copy(w_hi[:, 0].rearrange("p k o -> p (k o)"), ps[:, A_BANK, :]).then_inc(w_hi_done[0], 1)
            act.wait_ge(w_T[1], 1)
            scaled(w_hi, 1).then_inc(w_hi_done[1], 1)
            for l in (2, 3):
                act.wait_ge(w_T[l], 1)
                scaled(w_full, l).then_inc(w_full_done[l], 1)
            act.wait_ge(a_bias_done, 1)
            target0(0)
            act.wait_ge(w_T[4], 1)
            scaled(w_full, 4).then_inc(w_full_done[4], 1)
            for l in (2, 3, 4):
                scaled(w_hi, l).then_inc(w_hi_done[l], 1)
            act.wait_ge(head_T, 1)
            nc.scalar.copy(head_hi[:].rearrange("p k o -> p (k o)"), ps[:, HEADT_BANK, 0:HB * OUT]).then_inc(head_hi_done, 1)

            def tanh_columns(r):
                act.wait_ge(col_z, r)
                nc.scalar.activation(t_col[:, r:LAST, :], z_col[:, r:LAST, :], ACT.Tanh).then_inc(col_t, 1)

            keep_u(0)
            act.wait_ge(u_done, 1)

            address = act.alloc_register("address")

            def taken_after_wait(value, least, most):
                act.reg_mov(address, value)
                return act.snap(address, min_val=least, max_val=most)

            def layer(l, c, w, parity):
                n = wave_number(c, w)
                freed = sum_done if l == LAST else split_done[l]
                for o in range(HB):
                    if l > 1:
                        act.wait_ge(mm_done[l], 2 * n + o + 1)
                    if o == 0 and not (isinstance(n, int) and n < 2):
                        act.wait_ge(freed, n - 1)
                    source = u_sb[:, o, :] if l == 1 else ps[:, Z_BANK[l] + o, :]
                    if isinstance(w, int):
                        scale = RAMP[w] if l == 1 else DOWN[w]
                    else:
                        at = taken_after_wait(w, 1, WAVES - 1)
                        scale = (ramp_tab if l == 1 else down_tab)[:, bass.ds(at, 1)]
                    nc.scalar.activation(tgt[l][:, parity, o, :], source, ACT.Tanh, bias=bias[:, 1 + l, o:o + 1],
                                         scale=scale).then_inc(tanh_done[l], 1)

            def seam(prev, nxt):
                for i in range(SEAM if nxt is not None else LAGS):
                    for l in range(1, L):
                        w = i - (l - 1)
                        c, v = (nxt, w) if w >= 0 else (prev, w + WAVES)
                        if c is not None:
                            layer(l, c, v, v % 2)
                    if prev is None and i + 1 < LAST:
                        tanh_columns(i + 1)

            def steady(c, end):
                with act.Fori(SEAM, end - 1, 2) as m:
                    for i in range(2):
                        for l in range(1, L):
                            layer(l, c, m + (i - (l - 1)), (i - (l - 1)) % 2)

            def ahead(c):
                for i in range(AHEAD):
                    for l in range(1, L):
                        w = WAVES - AHEAD + i - (l - 1)
                        layer(l, c, w, w % 2)
                    if i == 1:
                        act.wait_ge(xT_mm, c + 2)
                        x_high()
                    elif i == 3:
                        target0(c + 1)
                act.wait_ge(tanh_done[1], HB * wave_number(c, WAVES))
                keep_u(c + 1)
                act.wait_ge(u_done, c + 2)

            seam(None, 0)
            act.wait_ge(tab_step, 2)
            with act.Fori(0, NCH - 1) as c:
                steady(c, WAVES - AHEAD)
                ahead(c)
                seam(c, c + 1)
            steady(NCH - 1, WAVES)
            seam(NCH - 1, None)

        @block.vector
        def _(dve):
            def x_low(c):
                dve.wait_ge(xT_hi_done, c + 1)
                nc.vector.tensor_tensor(xT_lo[:], ps[:, SETUP_BANK:SETUP_BANK + HB, :], xT_hi[:].bitcast(f32),
                                        ALU.subtract).then_inc(xT_done, 1)

            def split_t0(c):
                dve.wait_ge(t0_tanh, c + 1)
                nc.vector.tensor_copy(t0_hi[:], t0[:]).then_inc(t0_hi_done, 1)
                dve.wait_ge(t0_hi_done, c + 1)
                nc.vector.tensor_tensor(t0_lo[:], t0[:], t0_hi[:].bitcast(f32), ALU.subtract).then_inc(t0_done, 1)

            def weight_low(l):
                dve.wait_ge(w_hi_done[l], 1)
                nc.vector.scalar_tensor_tensor(
                    out=w_lo[:, l].rearrange("p k o -> p (k o)"), in0=ps[:, W_BANK[l], :], scalar=w_scale[:, l:l + 1],
                    in1=w_hi[:, l].rearrange("p k o -> p (k o)").bitcast(f32), op0=ALU.mult,
                    op1=ALU.subtract).then_inc(w_lo_done[l], 1)

            def column_input(r):
                dve.wait_ge(col_mm, r)
                nc.vector.scalar_tensor_tensor(
                    out=z_col[:, r:LAST, :].rearrange("p l b -> p (l b)"),
                    in0=ps[:, COL_BANK, r * HB:LAST * HB], scalar=HALF,
                    in1=bias[:, r + 2:L + 1, :].rearrange("p l b -> p (l b)"), op0=ALU.mult,
                    op1=ALU.add).then_inc(col_z, 1)

            def column_h(l):
                nc.vector.tensor_scalar(h_col[:, l - 1, :], g_col[:, l - 1, :], HALF, None, ALU.mult).then_inc(h_col_ready, 1)

            def column_step(r):
                dve.wait_ge(col_t, r + 1)
                nc.vector.scalar_tensor_tensor(out=g_col[:, r:LAST, :], in0=g_col[:, r:LAST, :], scalar=HALF,
                                               in1=t_col[:, r:LAST, :], op0=ALU.mult, op1=ALU.add).then_inc(col_g, 1)

            for w in range(WAVES):
                last = nc.vector.memset(up_tab[:, w:w + 1], UP[w])
            last.then_inc(tab_step, 1)
            for w in range(WAVES):
                nc.vector.memset(down_tab[:, w:w + 1], DOWN[w])
                last = nc.vector.memset(ramp_tab[:, w:w + 1], RAMP[w])
            last.then_inc(tab_step, 1)
            x_low(0)
            dve.wait_ge(w_hi_done[0], 1)
            nc.vector.tensor_tensor(w_lo[:, 0].rearrange("p k o -> p (k o)"), ps[:, A_BANK, :],
                                    w_hi[:, 0].rearrange("p k o -> p (k o)").bitcast(f32),
                                    ALU.subtract).then_inc(w_lo_done[0], 1)
            dve.wait_ge(a_mm, 2)
            dve.wait_ge(bias_ready, 1)
            nc.vector.tensor_tensor(a_bias[:], ps[:, BIAS_BANK, A_BIAS_AT:A_BIAS_AT + HB], bias[:, 1, :],
                                    ALU.add).then_inc(a_bias_done, 1)
            dve.wait_ge(scale_in, 16)
            weight_low(1)
            split_t0(0)
            for l in (2, 3, 4):
                weight_low(l)
            dve.wait_ge(head_hi_done, 1)
            nc.vector.tensor_tensor(head_lo[:].rearrange("p k o -> p (k o)"), ps[:, HEADT_BANK, 0:HB * OUT],
                                    head_hi[:].rearrange("p k o -> p (k o)").bitcast(f32),
                                    ALU.subtract).then_inc(head_lo_done, 1)
            dve.wait_ge(col_t, 1)
            column_h(1)
            dve.wait_ge(tab_step, 2)

            def split(l, c, w, up, first, parity):
                n = wave_number(c, w)
                t = tgt[l][:, parity]
                dve.wait_ge(tanh_done[l], 2 * n + 2)
                if not (isinstance(n, int) and n < 2):
                    dve.wait_ge(mm_done[l + 1], 2 * n - 2)
                if first:
                    dve.wait_ge(h_col_ready, l)
                    for o in range(HB):
                        last = nc.vector.tensor_scalar(t[:, o, :], t[:, o, :], h_col[:, l - 1, o:o + 1], None, ALU.add)
                    last.then_inc(first_done, 1)
                    dve.wait_ge(first_done, c * (LAST - 1) + l)
                nc.vector.tensor_scalar(t_hi[l][:, parity], t, up, None, ALU.mult).then_inc(hi_part[l], 1)
                dve.wait_ge(hi_part[l], n + 1)
                nc.vector.scalar_tensor_tensor(out=t_lo[l][:, parity], in0=t, scalar=up,
                                               in1=t_hi[l][:, parity].bitcast(f32), op0=ALU.mult,
                                               op1=ALU.subtract).then_inc(split_done[l], 1)

            def add_target(c, w, up, first, parity):
                n = wave_number(c, w)
                t = tgt[LAST][:, parity]
                dve.wait_ge(tanh_done[LAST], 2 * n + 2)
                if first:
                    dve.wait_ge(h_col_ready, LAST)
                    if not (isinstance(c, int) and c == 0):
                        dve.wait_ge(h4_done, HB * c)
                    for o in range(HB):
                        last = nc.vector.tensor_scalar(g4[:, o, :], t[:, o, :], h_col[:, LAST - 1, o:o + 1], up,
                                                       ALU.add, ALU.mult)
                    last.then_inc(sum_done, 1)
                else:
                    dve.wait_ge(sum_done, n)
                    nc.vector.scalar_tensor_tensor(out=g4[:], in0=t, scalar=up, in1=g4[:], op0=ALU.mult,
                                                   op1=ALU.add).then_inc(sum_done, 1)

            def split_h4(c, with_last_wave):
                if not with_last_wave:
                    dve.wait_ge(sum_done, wave_number(c, WAVES))
                for o in range(HB):
                    if with_last_wave:
                        n = wave_number(c, WAVES - 1)
                        dve.wait_ge(tanh_done[LAST], 2 * n + o + 1)
                        dve.wait_ge(sum_done, n + o)
                        nc.vector.scalar_tensor_tensor(
                            out=g4[:, o, :], in0=tgt[LAST][:, (WAVES - 1) % 2, o, :], scalar=UP[-1], in1=g4[:, o, :],
                            op0=ALU.mult, op1=ALU.add).then_inc(sum_done, 1)
                        dve.wait_ge(sum_done, n + o + 1)
                    nc.vector.tensor_scalar(h4_hi[:, o, :], g4[:, o, :], HALF, None, ALU.mult).then_inc(h4_hi_done, 1)
                    dve.wait_ge(h4_hi_done, HB * c + o + 1)
                    nc.vector.scalar_tensor_tensor(out=h4_lo[:, o, :], in0=g4[:, o, :], scalar=HALF,
                                                   in1=h4_hi[:, o, :].bitcast(f32), op0=ALU.mult,
                                                   op1=ALU.subtract).then_inc(h4_done, 1)

            def write_y(c):
                dve.wait_ge(y_mm, c + 1)
                nc.vector.tensor_tensor(y_sb[:, bass.ds(c, 1)].rearrange("p a n o -> p (a n) o"),
                                        ps[:, HEAD_BANK, :].rearrange("p (n o) -> p n o", o=OUT),
                                        b_head_all[:].unsqueeze(1).broadcast_to([P, TPC, OUT]),
                                        ALU.add).then_inc(y_done, 1)

            def wave(l, c, w, up, first, parity):
                if l == LAST:
                    add_target(c, w, up, first, parity)
                else:
                    split(l, c, w, up, first, parity)

            def seam(prev, nxt):
                for i in range(SEAM if nxt is not None else LAGS):
                    for l in range(1, L):
                        w = i - (l - 1)
                        c, v = (nxt, w) if w >= 0 else (prev, w + WAVES)
                        if l == LAST and i == LAGS and prev is not None:
                            split_h4(prev, False)
                        if c is not None and not (nxt is None and l == LAST and v == WAVES - 1):
                            wave(l, c, v, UP[v], v == 0, v % 2)
                    if prev is None and i + 1 < LAST:
                        column_input(i + 1)
                        column_step(i + 1)
                        dve.wait_ge(col_g, i + 1)
                        column_h(i + 2)
                if nxt is None:
                    split_h4(prev, True)
                if prev is not None:
                    write_y(prev)

            def steady(c, end):
                with dve.Fori(SEAM, end - 1, 2) as m:
                    for i in range(2):
                        for l in range(1, L):
                            w = m + (i - (l - 1))
                            wave(l, c, w, up_tab[:, bass.ds(w, 1)], False, (i - (l - 1)) % 2)

            def ahead(c):
                for i in range(AHEAD):
                    for l in range(1, L):
                        w = WAVES - AHEAD + i - (l - 1)
                        wave(l, c, w, UP[w], False, w % 2)
                    if i == 1:
                        x_low(c + 1)
                    elif i == 3:
                        split_t0(c + 1)

            seam(None, 0)
            dve.wait_ge(b_head_in, 16)
            with dve.Fori(0, NCH - 1) as c:
                steady(c, WAVES - AHEAD)
                ahead(c)
                seam(c, c + 1)
            steady(NCH - 1, WAVES)
            seam(NCH - 1, None)


_INS = ['r_x', 'L0_rec_W_in', 'L0_rec_b_in', 'L0_rec_Ws', 'L0_rec_bs', 'L0_rec_scales', 'L0_rec_W_head', 'L0_rec_b_head']
_OUTS = [((2048, 128), 'float32')]


def kernel(**inputs):
    import numpy as _np
    import concourse.bacc as _bacc
    from concourse import mybir as _mybir
    from concourse.bass_utils import run_bass_kernel_spmd as _run

    nc = _bacc.Bacc("TRN2", target_bir_lowering=False, num_devices=1)
    arrays, args = {}, []
    for name in _INS:
        a = _np.ascontiguousarray(inputs[name])
        arrays[f"in_{name}_dram"] = a
        args.append(nc.dram_tensor(f"in_{name}_dram", a.shape, _mybir.dt.from_np(a.dtype), kind="ExternalInput").ap())
    for i, (shape, dtype) in enumerate(_OUTS):
        dt = _mybir.dt.from_np(_np.dtype(dtype))
        args.append(nc.dram_tensor(f"out_{i}_dram", shape, dt, kind="ExternalOutput").ap())
    leaky_tanh_stack(nc, *args)
    r = _run(nc, [arrays], core_ids=[0])
    return r.results[0]["out_0_dram"]
```

```python
from contextlib import ExitStack

import concourse.bass as bass
from concourse import mybir


def leaky_tanh_stack(nc: bass.Bass, x, W_in, b_in, Ws, bs, scales, W_head, b_head, y):
    f32, f32r = mybir.dt.float32, mybir.dt.float32r
    ALU, ACT = mybir.AluOpType, mybir.ActivationFunctionType

    P = 128
    ROWS, IN = x.shape
    L, H, _ = Ws.shape
    OUT = W_head.shape[0]
    STEPS = 30
    HB = H // P
    CH = 512
    NCH = ROWS // CH
    TPC = CH // P
    LAST = L - 1
    WAVES = STEPS - LAST
    SEAM = 6
    AHEAD = 6
    LAGS = LAST - 1
    assert IN == H and OUT == P and LAST == 4 and WAVES % 2 == 0 and SEAM % 2 == 0
    HALF = 0.5
    UP = [2.0 ** (w - WAVES + 1) for w in range(WAVES)]
    DOWN = [2.0 ** (WAVES - 2 - w) for w in range(WAVES)]
    RAMP = [1.0 - 2.0 ** -(w + 1) for w in range(WAVES)]

    ctx = ExitStack()
    with ctx:
        def sb(name, shape, dt=f32):
            return ctx.enter_context(nc.sbuf_tensor(name, shape, dt))

        def sem(name):
            return ctx.enter_context(nc.semaphore(name))

        ident = sb("ident", [P, P])
        w_in_rows = sb("w_in_rows", [P, HB, IN])
        w_rows = sb("w_rows", [P, L, HB, H])
        head_rows = sb("head_rows", [P, H])
        bias_rows = sb("bias_rows", [(L + 1) * HB, P])
        bias = sb("bias", [P, L + 1, HB])
        b_head_all = sb("b_head_all", [P, OUT])
        a_bias = sb("a_bias", [P, HB])
        w_scale = sb("w_scale", [P, L])
        w_hi = sb("w_hi", [P, L, HB, H], f32r)
        w_lo = sb("w_lo", [P, L, HB, H], f32r)
        w_full = sb("w_full", [P, L, HB, H])
        head_hi = sb("head_hi", [P, HB, OUT], f32r)
        head_lo = sb("head_lo", [P, HB, OUT], f32r)
        x_rows = sb("x_rows", [P, TPC, IN])
        xT_hi = sb("xT_hi", [P, HB, CH], f32r)
        xT_lo = sb("xT_lo", [P, HB, CH], f32r)
        t0 = sb("t0", [P, HB, CH])
        t0_hi = sb("t0_hi", [P, HB, CH], f32r)
        t0_lo = sb("t0_lo", [P, HB, CH], f32r)
        u_sb = sb("u_sb", [P, HB, CH])
        up_tab = sb("up_tab", [P, WAVES])
        down_tab = sb("down_tab", [P, WAVES])
        ramp_tab = sb("ramp_tab", [P, WAVES])
        g_col = sb("g_col", [P, LAST, HB])
        z_col = sb("z_col", [P, LAST, HB])
        t_col = sb("t_col", [P, LAST, HB])
        h_col = sb("h_col", [P, LAST, HB])
        tgt = [None] + [sb(f"tgt{l}", [P, 2, HB, CH]) for l in range(1, L)]
        t_hi = [None] + [sb(f"t_hi{l}", [P, 2, HB, CH], f32r) for l in range(1, LAST)]
        t_lo = [None] + [sb(f"t_lo{l}", [P, 2, HB, CH], f32r) for l in range(1, LAST)]
        g4 = sb("g4", [P, HB, CH])
        h4_hi = sb("h4_hi", [P, HB, CH], f32r)
        h4_lo = sb("h4_lo", [P, HB, CH], f32r)
        y_sb = sb("y_sb", [P, NCH, TPC, OUT])

        ps = ctx.enter_context(nc.psum_tensor("ps", [P, 8, CH], f32))
        Z_BANK = {2: 2, 3: 4, 4: 6}
        HEAD_BANK = 0
        SETUP_BANK = 0
        BIAS_BANK, A_BANK, HEADT_BANK = 2, 4, 5
        W_BANK = [3, 5, 7, 2, 3]
        A_BIAS_AT = 64
        COL_BANK = 1

        w_rows_in = [sem(f"w_rows_in{l}") for l in range(L)]
        w_in_rows_in = sem("w_in_rows_in")
        head_rows_in = sem("head_rows_in")
        bias_rows_in = sem("bias_rows_in")
        scale_in = sem("scale_in")
        b_head_in = sem("b_head_in")
        x_in = sem("x_in")
        y_stored = sem("y_stored")
        ident_zeroed = sem("ident_zeroed")
        ident_ready = sem("ident_ready")
        tab_ready = sem("tab_ready")
        bias_T = sem("bias_T")
        bias_ready = sem("bias_ready")
        w_T = [sem(f"w_T{l}") for l in range(L)]
        head_T = sem("head_T")
        w_full_done = [sem(f"w_full_done{l}") for l in range(L)]
        w_hi_done = [sem(f"w_hi_done{l}") for l in range(L)]
        w_lo_done = [sem(f"w_lo_done{l}") for l in range(L)]
        head_hi_done = sem("head_hi_done")
        head_lo_done = sem("head_lo_done")
        a_mm = sem("a_mm")
        a_bias_done = sem("a_bias_done")
        col_mm = sem("col_mm")
        col_z = sem("col_z")
        col_t = sem("col_t")
        col_g = sem("col_g")
        h_col_ready = sem("h_col_ready")
        xT_mm = sem("xT_mm")
        xT_hi_done = sem("xT_hi_done")
        xT_done = sem("xT_done")
        t0_mm = sem("t0_mm")
        t0_tanh = sem("t0_tanh")
        t0_hi_done = sem("t0_hi_done")
        t0_done = sem("t0_done")
        u_mm = sem("u_mm")
        u_done = sem("u_done")
        tanh_done = [None] + [sem(f"tanh_done{l}") for l in range(1, L)]
        hi_part = [None] + [sem(f"hi_part{l}") for l in range(1, LAST)]
        first_done = sem("first_done")
        split_done = [None] + [sem(f"split_done{l}") for l in range(1, LAST)]
        sum_done = sem("sum_done")
        mm_done = {l: sem(f"mm_done{l}") for l in range(2, L)}
        h4_hi_done = sem("h4_hi_done")
        h4_done = sem("h4_done")
        y_mm = sem("y_mm")
        y_done = sem("y_done")

        def passes_of_half(out, weights_hi, weights_lo, moving_hi, moving_lo, o, k, start):
            cols = slice(o * P, (o + 1) * P)
            ops = [(weights_hi, moving_lo), (weights_hi, moving_hi), (weights_lo, moving_hi)]
            for i, (w, v) in enumerate(ops):
                last = nc.tensor.matmul(out, w[:, k, cols], v[:, k, :], start=(start and k == 0 and i == 0),
                                        stop=(k == HB - 1 and i == len(ops) - 1), skip_group_check=True)
            return last

        def passes(out, weights_hi, weights_lo, moving_hi, moving_lo, o, start):
            for k in range(HB):
                last = passes_of_half(out, weights_hi, weights_lo, moving_hi, moving_lo, o, k, start)
            return last

        def wave_number(c, w):
            return c * WAVES + w

        block = ctx.enter_context(nc.Block())

        @block.sync
        def _(sp):
            def load_matrix(l):
                sp.dma_start(w_rows[:, l], Ws[l].rearrange("(b p) i -> p b i", p=P)).then_inc(w_rows_in[l], 16)

            def load_x(c):
                if c > 0:
                    sp.wait_ge(xT_mm, c)
                sp.dma_start(x_rows[:], x[c * CH:(c + 1) * CH, :].rearrange("(n p) i -> p n i", p=P)).then_inc(x_in, 16)

            def store_y(c):
                sp.wait_ge(y_done, c + 1)
                sp.dma_start(y[c * CH:(c + 1) * CH, :].rearrange("(n p) o -> p n o", p=P),
                             y_sb[:, c]).then_inc(y_stored, 16)

            load_matrix(0)
            sp.dma_start(w_in_rows[:], W_in.rearrange("(b p) i -> p b i", p=P)).then_inc(w_in_rows_in, 16)
            load_x(0)
            for l in range(1, L):
                load_matrix(l)
            sp.dma_start(head_rows[:], W_head).then_inc(head_rows_in, 16)
            sp.dma_start(b_head_all[:], b_head.rearrange("(a o) -> a o", a=1).broadcast_to([P, OUT])
                         ).then_inc(b_head_in, 16)
            load_x(1)
            for c in range(NCH):
                if c + 2 < NCH:
                    load_x(c + 2)
                store_y(c)
            sp.wait_ge(y_stored, 16 * NCH)

        @block.gpsimd
        def _(pool):
            nc.gpsimd.memset(ident[:], 0.0).then_inc(ident_zeroed, 1)
            pool.wait_ge(ident_zeroed, 1)
            nc.gpsimd.affine_select(out=ident[:], in_=ident[:], compare_op=ALU.not_equal, fill=1.0, base=0,
                                    pattern=[[-1, P]], channel_multiplier=1).then_inc(ident_ready, 1)
            for w in range(WAVES):
                nc.gpsimd.memset(up_tab[:, w:w + 1], UP[w])
                nc.gpsimd.memset(down_tab[:, w:w + 1], DOWN[w])
                last = nc.gpsimd.memset(ramp_tab[:, w:w + 1], RAMP[w])
            last.then_inc(tab_ready, 1)

        @block.tensor
        def _(pe):
            def transpose_matrix(l):
                pe.wait_ge(w_rows_in[l], 16)
                for k in range(HB):
                    for o in range(HB):
                        at = k * H + o * P
                        last = nc.tensor.transpose(ps[:, W_BANK[l], at:at + P],
                                                   w_rows[:, l, o, k * P:(k + 1) * P], ident[:])
                last.then_inc(w_T[l], 1)

            def shared_columns(r):
                if r == 1:
                    pe.wait_ge(col_t, 1)
                    pe.wait_ge(u_done, 1)
                else:
                    pe.wait_ge(col_g, r - 1)
                for l in range(r + 1, LAST + 1):
                    for o in range(HB):
                        at = (l - 1) * HB + o
                        for k in range(HB):
                            last = nc.tensor.matmul(ps[:, COL_BANK, at:at + 1],
                                                    w_full[:, l, k, o * P:(o + 1) * P],
                                                    g_col[:, l - 2, k:k + 1], start=(k == 0), stop=(k == HB - 1))
                last.then_inc(col_mm, 1)

            def transpose_x(c):
                pe.wait_ge(x_in, 16 * c + 16)
                for k in range(HB):
                    for n in range(TPC):
                        last = nc.tensor.transpose(ps[:, SETUP_BANK + k, n * P:(n + 1) * P],
                                                   x_rows[:, n, k * P:(k + 1) * P], ident[:])
                last.then_inc(xT_mm, 1)

            def product_t0(c):
                pe.wait_ge(xT_done, c + 1)
                for o in range(HB):
                    for k in range(HB):
                        if o == 0 and isinstance(c, int) and c == 0:
                            pe.wait_ge(w_lo_done[0], k + 1)
                        last = passes_of_half(ps[:, SETUP_BANK + o, :], w_hi[:, 0], w_lo[:, 0], xT_hi, xT_lo, o, k, True)
                    last.then_inc(t0_mm, 1)

            def product_u(c):
                for o in range(HB):
                    for k in range(HB):
                        if o == 0:
                            pe.wait_ge(t0_done, HB * c + k + 1)
                        last = passes_of_half(ps[:, SETUP_BANK + o, :], w_hi[:, 1], w_lo[:, 1], t0_hi, t0_lo, o, k, True)
                last.then_inc(u_mm, 1)

            pe.wait_ge(ident_ready, 1)
            pe.wait_ge(bias_rows_in, 32)
            NB = (L + 1) * HB
            nc.tensor.transpose(ps[:, BIAS_BANK, 0:NB], bias_rows[:], ident[0:NB, 0:NB]).then_inc(bias_T, 1)
            transpose_matrix(0)
            transpose_x(0)
            transpose_matrix(1)
            pe.wait_ge(w_full_done[0], 1)
            pe.wait_ge(w_in_rows_in, 16)
            for i in range(HB):
                for k in range(HB):
                    last = nc.tensor.matmul(ps[:, A_BANK + 2 * i, 0:H], w_in_rows[:, k, i * P:(i + 1) * P],
                                            w_full[:, 0, k, :], start=(k == 0), stop=(k == HB - 1))
                last.then_inc(a_mm, 1)
            pe.wait_ge(bias_ready, 1)
            for o in range(HB):
                for k in range(HB):
                    last = nc.tensor.matmul(ps[:, BIAS_BANK, A_BIAS_AT + o:A_BIAS_AT + o + 1],
                                            w_full[:, 0, k, o * P:(o + 1) * P], bias[:, 0, k:k + 1],
                                            start=(k == 0), stop=(k == HB - 1))
            last.then_inc(a_mm, 1)
            transpose_matrix(2)
            product_t0(0)
            pe.wait_ge(a_bias_done, 1)
            transpose_matrix(3)
            transpose_matrix(4)
            pe.wait_ge(w_lo_done[1], 1)
            pe.wait_ge(head_rows_in, 16)
            for k in range(HB):
                last = nc.tensor.transpose(ps[:, HEADT_BANK, k * OUT:(k + 1) * OUT],
                                           head_rows[:, k * P:(k + 1) * P], ident[:])
            last.then_inc(head_T, 1)
            product_u(0)
            for l in range(2, L):
                pe.wait_ge(w_full_done[l], 1)
            shared_columns(1)
            for l in range(2, L):
                pe.wait_ge(w_lo_done[l], 1)
            pe.wait_ge(head_lo_done, 1)

            def layer(l, c, w, first, parity):
                n = wave_number(c, w)
                pe.wait_ge(split_done[l - 1], n + 1)
                for o in range(HB):
                    if not (isinstance(n, int) and n == 0):
                        pe.wait_ge(tanh_done[l], 2 * n + o - 1)
                    passes(ps[:, Z_BANK[l] + o, :], w_hi[:, l], w_lo[:, l], t_hi[l - 1][:, parity],
                           t_lo[l - 1][:, parity], o, first).then_inc(mm_done[l], 1)

            def head(c):
                for k in range(HB):
                    pe.wait_ge(h4_done, HB * c + k + 1)
                    for n in range(TPC):
                        rows = slice(n * P, (n + 1) * P)
                        ops = [(h4_hi[:, k, rows], head_lo[:, k, :]), (h4_hi[:, k, rows], head_hi[:, k, :]),
                               (h4_lo[:, k, rows], head_hi[:, k, :])]
                        for j, (a, b) in enumerate(ops):
                            last = nc.tensor.matmul(ps[:, HEAD_BANK, n * OUT:(n + 1) * OUT], a, b,
                                                    start=(k == 0 and n == 0 and j == 0),
                                                    stop=(k == HB - 1 and j == len(ops) - 1), skip_group_check=True)
                last.then_inc(y_mm, 1)

            def seam(prev, nxt):
                for i in range(SEAM if nxt is not None else LAGS):
                    for l in range(2, L):
                        w = i - (l - 2)
                        if w >= 0 and nxt is not None:
                            layer(l, nxt, w, w == 0, w % 2)
                        elif w < 0 and prev is not None:
                            layer(l, prev, w + WAVES, False, w % 2)
                    if prev is None and i + 2 < LAST:
                        shared_columns(i + 2)
                    if i == LAGS and prev is not None:
                        head(prev)
                if nxt is None:
                    head(prev)

            def steady(c, end):
                with pe.Fori(SEAM, end - 1, 2) as m:
                    for i in range(2):
                        for l in range(2, L):
                            layer(l, c, m + (i - (l - 2)), False, (i - (l - 2)) % 2)

            def ahead(c):
                for i in range(AHEAD):
                    for l in range(2, L):
                        w = WAVES - AHEAD + i - (l - 2)
                        layer(l, c, w, False, w % 2)
                    if i == 0:
                        transpose_x(c + 1)
                    elif i == 2:
                        product_t0(c + 1)
                    elif i == 4:
                        product_u(c + 1)

            seam(None, 0)
            with pe.Fori(0, NCH - 1) as c:
                steady(c, WAVES - AHEAD)
                ahead(c)
                seam(c, c + 1)
            steady(NCH - 1, WAVES)
            seam(NCH - 1, None)

        @block.scalar
        def _(act):
            act.dma_start(w_scale[:], scales.rearrange("(a l) -> a l", a=1).broadcast_to([P, L])).then_inc(scale_in, 16)
            act.dma_start(bias_rows[0:HB, :], b_in.rearrange("(b p) -> b p", p=P)).then_inc(bias_rows_in, 16)
            act.dma_start(bias_rows[HB:(L + 1) * HB, :],
                          bs.rearrange("l (b p) -> (l b) p", p=P)).then_inc(bias_rows_in, 16)
            nc.scalar.preload_act_table(ACT.Tanh)

            def scaled(out, l):
                return nc.scalar.mul(out[:, l].rearrange("p k o -> p (k o)"), ps[:, W_BANK[l], :], w_scale[:, l:l + 1])

            def x_high():
                return nc.scalar.copy(xT_hi[:].rearrange("p b n -> p (b n)"),
                                      ps[:, SETUP_BANK:SETUP_BANK + HB, :].rearrange("p b n -> p (b n)")
                                      ).then_inc(xT_hi_done, 1)

            def target0(c):
                for o in range(HB):
                    act.wait_ge(t0_mm, HB * c + o + 1)
                    nc.scalar.activation(t0[:, o, :], ps[:, SETUP_BANK + o, :], ACT.Tanh,
                                         bias=a_bias[:, o:o + 1]).then_inc(t0_tanh, 1)

            def keep_u(c):
                act.wait_ge(u_mm, c + 1)
                nc.scalar.copy(u_sb[:].rearrange("p b n -> p (b n)"),
                               ps[:, SETUP_BANK:SETUP_BANK + HB, :].rearrange("p b n -> p (b n)")).then_inc(u_done, 1)

            act.wait_ge(bias_T, 1)
            nc.scalar.copy(bias[:].rearrange("p m b -> p (m b)"), ps[:, BIAS_BANK, 0:(L + 1) * HB]).then_inc(bias_ready, 1)
            act.wait_ge(scale_in, 16)
            act.wait_ge(w_T[0], 1)
            scaled(w_full, 0).then_inc(w_full_done[0], 1)
            act.wait_ge(bias_ready, 1)
            nc.scalar.activation(g_col[:], bias[:, 2:L + 1, :], ACT.Tanh).then_inc(col_t, 1)
            act.wait_ge(xT_mm, 1)
            x_high()
            for k in range(HB):
                act.wait_ge(a_mm, k + 1)
                nc.scalar.copy(w_hi[:, 0, k, :], ps[:, A_BANK + 2 * k, 0:H]).then_inc(w_hi_done[0], 1)
            act.wait_ge(w_T[1], 1)
            scaled(w_hi, 1).then_inc(w_hi_done[1], 1)
            act.wait_ge(w_T[2], 1)
            scaled(w_full, 2).then_inc(w_full_done[2], 1)
            act.wait_ge(a_bias_done, 1)
            target0(0)
            for l in (3, 4):
                act.wait_ge(w_T[l], 1)
                scaled(w_full, l).then_inc(w_full_done[l], 1)
            for l in (2, 3, 4):
                scaled(w_hi, l).then_inc(w_hi_done[l], 1)
            act.wait_ge(head_T, 1)
            nc.scalar.copy(head_hi[:].rearrange("p k o -> p (k o)"), ps[:, HEADT_BANK, 0:HB * OUT]).then_inc(head_hi_done, 1)

            def tanh_columns(r):
                act.wait_ge(col_z, r)
                nc.scalar.activation(t_col[:, r:LAST, :], z_col[:, r:LAST, :], ACT.Tanh).then_inc(col_t, 1)

            act.wait_ge(u_mm, 1)
            address = act.alloc_register("address")

            def taken_after_wait(value, least, most):
                act.reg_mov(address, value)
                return act.snap(address, min_val=least, max_val=most)

            def layer(l, c, w, parity):
                n = wave_number(c, w)
                freed = sum_done if l == LAST else split_done[l]
                for o in range(HB):
                    if l > 1:
                        act.wait_ge(mm_done[l], 2 * n + o + 1)
                    if o == 0 and not (isinstance(n, int) and n < 2):
                        act.wait_ge(freed, n - 1)
                    if l == 1:
                        source = ps[:, SETUP_BANK + o, :] if isinstance(n, int) and n == 0 else u_sb[:, o, :]
                    else:
                        source = ps[:, Z_BANK[l] + o, :]
                    if isinstance(w, int):
                        scale = RAMP[w] if l == 1 else DOWN[w]
                    else:
                        at = taken_after_wait(w, 1, WAVES - 1)
                        scale = (ramp_tab if l == 1 else down_tab)[:, bass.ds(at, 1)]
                    nc.scalar.activation(tgt[l][:, parity, o, :], source, ACT.Tanh, bias=bias[:, 1 + l, o:o + 1],
                                         scale=scale).then_inc(tanh_done[l], 1)

            def high_part(c, w, parity):
                n = wave_number(c, w)
                act.wait_ge(tanh_done[1], 2 * n + 2)
                if not (isinstance(n, int) and n < 2):
                    act.wait_ge(mm_done[2], 2 * n - 2)
                up = UP[w] if isinstance(w, int) else up_tab[:, bass.ds(taken_after_wait(w, 1, WAVES - 1), 1)]
                nc.scalar.mul(t_hi[1][:, parity].rearrange("p b n -> p (b n)"),
                              tgt[1][:, parity].rearrange("p b n -> p (b n)"), up).then_inc(hi_part[1], 1)

            def seam(prev, nxt):
                for i in range(SEAM if nxt is not None else LAGS):
                    for l in range(1, L):
                        w = i - (l - 1)
                        c, v = (nxt, w) if w >= 0 else (prev, w + WAVES)
                        if c is not None:
                            layer(l, c, v, v % 2)
                        if l == 2 and i > 0 and nxt is not None and prev is not None:
                            high_part(nxt, i, i % 2)
                    if prev is None and i == 0:
                        keep_u(0)
                        act.wait_ge(u_done, 1)
                    if prev is None and i + 1 < LAST:
                        tanh_columns(i + 1)

            def steady(c, end):
                with act.Fori(SEAM, end - 1, 2) as m:
                    for i in range(2):
                        for l in range(1, L):
                            layer(l, c, m + (i - (l - 1)), (i - (l - 1)) % 2)
                            if l == 2:
                                high_part(c, m + i, i)

            def ahead(c):
                for i in range(AHEAD):
                    for l in range(1, L):
                        w = WAVES - AHEAD + i - (l - 1)
                        layer(l, c, w, w % 2)
                        if l == 2:
                            high_part(c, w + 1, (w + 1) % 2)
                    if i == 1:
                        act.wait_ge(xT_mm, c + 2)
                        x_high()
                    elif i == 3:
                        target0(c + 1)
                act.wait_ge(tanh_done[1], HB * wave_number(c, WAVES))
                keep_u(c + 1)
                act.wait_ge(u_done, c + 2)

            seam(None, 0)
            act.wait_ge(tab_ready, 1)
            with act.Fori(0, NCH - 1) as c:
                steady(c, WAVES - AHEAD)
                ahead(c)
                seam(c, c + 1)
            steady(NCH - 1, WAVES)
            seam(NCH - 1, None)

        @block.vector
        def _(dve):
            def x_low(c):
                dve.wait_ge(xT_hi_done, c + 1)
                nc.vector.tensor_tensor(xT_lo[:], ps[:, SETUP_BANK:SETUP_BANK + HB, :], xT_hi[:].bitcast(f32),
                                        ALU.subtract).then_inc(xT_done, 1)

            def split_t0(c):
                for o in range(HB):
                    dve.wait_ge(t0_tanh, HB * c + o + 1)
                    nc.vector.tensor_copy(t0_hi[:, o], t0[:, o]).then_inc(t0_hi_done, 1)
                    dve.wait_ge(t0_hi_done, HB * c + o + 1)
                    nc.vector.tensor_tensor(t0_lo[:, o], t0[:, o], t0_hi[:, o].bitcast(f32),
                                            ALU.subtract).then_inc(t0_done, 1)

            def weight_low(l):
                dve.wait_ge(w_hi_done[l], 1)
                nc.vector.scalar_tensor_tensor(
                    out=w_lo[:, l].rearrange("p k o -> p (k o)"), in0=ps[:, W_BANK[l], :], scalar=w_scale[:, l:l + 1],
                    in1=w_hi[:, l].rearrange("p k o -> p (k o)").bitcast(f32), op0=ALU.mult,
                    op1=ALU.subtract).then_inc(w_lo_done[l], 1)

            def column_input(r):
                dve.wait_ge(col_mm, r)
                nc.vector.scalar_tensor_tensor(
                    out=z_col[:, r:LAST, :].rearrange("p l b -> p (l b)"),
                    in0=ps[:, COL_BANK, r * HB:LAST * HB], scalar=HALF,
                    in1=bias[:, r + 2:L + 1, :].rearrange("p l b -> p (l b)"), op0=ALU.mult,
                    op1=ALU.add).then_inc(col_z, 1)

            def column_h(l):
                nc.vector.tensor_scalar(h_col[:, l - 1, :], g_col[:, l - 1, :], HALF, None, ALU.mult).then_inc(h_col_ready, 1)

            def column_step(r):
                dve.wait_ge(col_t, r + 1)
                nc.vector.scalar_tensor_tensor(out=g_col[:, r:LAST, :], in0=g_col[:, r:LAST, :], scalar=HALF,
                                               in1=t_col[:, r:LAST, :], op0=ALU.mult, op1=ALU.add).then_inc(col_g, 1)

            x_low(0)
            for k in range(HB):
                dve.wait_ge(w_hi_done[0], k + 1)
                nc.vector.tensor_tensor(w_lo[:, 0, k, :], ps[:, A_BANK + 2 * k, 0:H], w_hi[:, 0, k, :].bitcast(f32),
                                        ALU.subtract).then_inc(w_lo_done[0], 1)
            dve.wait_ge(a_mm, HB + 1)
            dve.wait_ge(bias_ready, 1)
            nc.vector.tensor_tensor(a_bias[:], ps[:, BIAS_BANK, A_BIAS_AT:A_BIAS_AT + HB], bias[:, 1, :],
                                    ALU.add).then_inc(a_bias_done, 1)
            dve.wait_ge(scale_in, 16)
            weight_low(1)
            split_t0(0)
            for l in (2, 3, 4):
                weight_low(l)
            dve.wait_ge(head_hi_done, 1)
            nc.vector.tensor_tensor(head_lo[:].rearrange("p k o -> p (k o)"), ps[:, HEADT_BANK, 0:HB * OUT],
                                    head_hi[:].rearrange("p k o -> p (k o)").bitcast(f32),
                                    ALU.subtract).then_inc(head_lo_done, 1)
            dve.wait_ge(col_t, 1)
            column_h(1)

            def split(l, c, w, up, first, parity, high_here):
                n = wave_number(c, w)
                t = tgt[l][:, parity]
                dve.wait_ge(tanh_done[l], 2 * n + 2)
                if not (isinstance(n, int) and n < 2):
                    dve.wait_ge(mm_done[l + 1], 2 * n - 2)
                if first:
                    dve.wait_ge(h_col_ready, l)
                    for o in range(HB):
                        last = nc.vector.tensor_scalar(t[:, o, :], t[:, o, :], h_col[:, l - 1, o:o + 1], None, ALU.add)
                    last.then_inc(first_done, 1)
                    dve.wait_ge(first_done, c * (LAST - 1) + l)
                if high_here:
                    nc.vector.tensor_scalar(t_hi[l][:, parity], t, up, None, ALU.mult).then_inc(hi_part[l], 1)
                dve.wait_ge(hi_part[l], n + 1)
                nc.vector.scalar_tensor_tensor(out=t_lo[l][:, parity], in0=t, scalar=up,
                                               in1=t_hi[l][:, parity].bitcast(f32), op0=ALU.mult,
                                               op1=ALU.subtract).then_inc(split_done[l], 1)

            def add_target(c, w, up, first, parity):
                n = wave_number(c, w)
                t = tgt[LAST][:, parity]
                dve.wait_ge(tanh_done[LAST], 2 * n + 2)
                if first:
                    dve.wait_ge(h_col_ready, LAST)
                    if not (isinstance(c, int) and c == 0):
                        dve.wait_ge(h4_done, HB * c)
                    for o in range(HB):
                        last = nc.vector.tensor_scalar(g4[:, o, :], t[:, o, :], h_col[:, LAST - 1, o:o + 1], up,
                                                       ALU.add, ALU.mult)
                    last.then_inc(sum_done, 1)
                else:
                    dve.wait_ge(sum_done, n)
                    nc.vector.scalar_tensor_tensor(out=g4[:], in0=t, scalar=up, in1=g4[:], op0=ALU.mult,
                                                   op1=ALU.add).then_inc(sum_done, 1)

            def split_h4(c, with_last_wave):
                if not with_last_wave:
                    dve.wait_ge(sum_done, wave_number(c, WAVES))
                for o in range(HB):
                    if with_last_wave:
                        n = wave_number(c, WAVES - 1)
                        dve.wait_ge(tanh_done[LAST], 2 * n + o + 1)
                        dve.wait_ge(sum_done, n + o)
                        nc.vector.scalar_tensor_tensor(
                            out=g4[:, o, :], in0=tgt[LAST][:, (WAVES - 1) % 2, o, :], scalar=UP[-1], in1=g4[:, o, :],
                            op0=ALU.mult, op1=ALU.add).then_inc(sum_done, 1)
                        dve.wait_ge(sum_done, n + o + 1)
                    nc.vector.tensor_scalar(h4_hi[:, o, :], g4[:, o, :], HALF, None, ALU.mult).then_inc(h4_hi_done, 1)
                    dve.wait_ge(h4_hi_done, HB * c + o + 1)
                    nc.vector.scalar_tensor_tensor(out=h4_lo[:, o, :], in0=g4[:, o, :], scalar=HALF,
                                                   in1=h4_hi[:, o, :].bitcast(f32), op0=ALU.mult,
                                                   op1=ALU.subtract).then_inc(h4_done, 1)

            def write_y(c):
                dve.wait_ge(y_mm, c + 1)
                nc.vector.tensor_tensor(y_sb[:, bass.ds(c, 1)].rearrange("p a n o -> p (a n) o"),
                                        ps[:, HEAD_BANK, :].rearrange("p (n o) -> p n o", o=OUT),
                                        b_head_all[:].unsqueeze(1).broadcast_to([P, TPC, OUT]),
                                        ALU.add).then_inc(y_done, 1)

            def wave(l, c, w, up, first, parity, start_up=False):
                if l == LAST:
                    add_target(c, w, up, first, parity)
                else:
                    split(l, c, w, up, first, parity, l > 1 or first or start_up)

            def seam(prev, nxt):
                for i in range(SEAM if nxt is not None else LAGS):
                    for l in range(1, L):
                        w = i - (l - 1)
                        c, v = (nxt, w) if w >= 0 else (prev, w + WAVES)
                        if l == LAST and i == LAGS and prev is not None:
                            split_h4(prev, False)
                        if c is not None and not (nxt is None and l == LAST and v == WAVES - 1):
                            wave(l, c, v, UP[v], v == 0, v % 2, prev is None)
                    if prev is None and i + 1 < LAST:
                        column_input(i + 1)
                        column_step(i + 1)
                        dve.wait_ge(col_g, i + 1)
                        column_h(i + 2)
                if nxt is None:
                    split_h4(prev, True)
                if prev is not None:
                    write_y(prev)

            def steady(c, end):
                with dve.Fori(SEAM, end - 1, 2) as m:
                    for i in range(2):
                        for l in range(1, L):
                            w = m + (i - (l - 1))
                            wave(l, c, w, up_tab[:, bass.ds(w, 1)], False, (i - (l - 1)) % 2)

            def ahead(c):
                for i in range(AHEAD):
                    for l in range(1, L):
                        w = WAVES - AHEAD + i - (l - 1)
                        wave(l, c, w, UP[w], False, w % 2)
                    if i == 1:
                        x_low(c + 1)
                    elif i == 3:
                        split_t0(c + 1)

            seam(None, 0)
            dve.wait_ge(b_head_in, 16)
            dve.wait_ge(tab_ready, 1)
            with dve.Fori(0, NCH - 1) as c:
                steady(c, WAVES - AHEAD)
                ahead(c)
                seam(c, c + 1)
            steady(NCH - 1, WAVES)
            seam(NCH - 1, None)


_INS = ['r_x', 'L0_rec_W_in', 'L0_rec_b_in', 'L0_rec_Ws', 'L0_rec_bs', 'L0_rec_scales', 'L0_rec_W_head', 'L0_rec_b_head']
_OUTS = [((2048, 128), 'float32')]


def kernel(**inputs):
    import numpy as _np
    import concourse.bacc as _bacc
    from concourse import mybir as _mybir
    from concourse.bass_utils import run_bass_kernel_spmd as _run

    nc = _bacc.Bacc("TRN2", target_bir_lowering=False, num_devices=1)
    arrays, args = {}, []
    for name in _INS:
        a = _np.ascontiguousarray(inputs[name])
        arrays[f"in_{name}_dram"] = a
        args.append(nc.dram_tensor(f"in_{name}_dram", a.shape, _mybir.dt.from_np(a.dtype), kind="ExternalInput").ap())
    for i, (shape, dtype) in enumerate(_OUTS):
        dt = _mybir.dt.from_np(_np.dtype(dtype))
        args.append(nc.dram_tensor(f"out_{i}_dram", shape, dt, kind="ExternalOutput").ap())
    leaky_tanh_stack(nc, *args)
    r = _run(nc, [arrays], core_ids=[0])
    return r.results[0]["out_0_dram"]
```
